# Optimizing a Trainium2 kernel written in Bass

```python
import numpy as np
import jax
import jax.numpy as jnp

def _softmax(x, axis=-1):
    return jax.nn.softmax(x, axis=axis)

def _gelu(x):
    return jax.nn.gelu(x, approximate=True)

def _silu(x):
    return jax.nn.silu(x)

def _sigmoid(x):
    return jax.nn.sigmoid(x)

def _layernorm(x, axis=-1, eps=1e-05):
    m = jnp.mean(x, axis=axis, keepdims=True)
    v = jnp.var(x, axis=axis, keepdims=True)
    return (x - m) / jnp.sqrt(v + eps)

def _scatter_add(tgt, idx, src, axis=0):
    return tgt.at[idx].add(src)

def _segment_sum(src, seg, n):
    return jax.ops.segment_sum(src, seg, n)
kernel_name = 'mk_adj_preln_d1_adj_r2_e262c9'

def setup_inputs(seed: int=0):
    np.random.seed(seed)
    _w = jnp.asarray

    def _rec_inputs():
        import jax
        import jax.numpy as jnp
        _gk = jax.random.key(seed)
        x = -0.0002422 + 1 * jax.random.normal(jax.random.fold_in(_gk, 1), (64, 128, 512), jnp.float32)
        _w = (1.0 + jnp.arange(128, dtype=jnp.float32)) ** (-0.5)
        _w = _w / _w.mean()
        _pij = jnp.clip(0.03125 * _w[:, None] * _w[None, :], 0.0, 1.0)
        _a = jax.random.uniform(jax.random.fold_in(_gk, 2), (64, 128, 128)) < _pij
        adj = _a.astype(jnp.int32)
        return (x, adj)
    x, adj = _rec_inputs()

    def _L0_gnn_setup():
        import jax, jax.numpy as jnp
        import numpy as np
        IN_DIM = 512
        OUT_DIM = 512
        BATCH = 128
        NUM_OBJS = 100
        key = jax.random.key(seed)
        k1, k2, k3, k4, k5 = jax.random.split(key, 5)
        stdv = 1.0 / np.sqrt(OUT_DIM)
        feature = jax.random.normal(k1, (BATCH, NUM_OBJS, IN_DIM), dtype=jnp.float32)
        graph = jax.random.randint(k2, (BATCH, NUM_OBJS, NUM_OBJS), 0, 2, dtype=jnp.int32)
        weight = jax.random.uniform(k3, (IN_DIM, OUT_DIM), dtype=jnp.float32, minval=-stdv, maxval=stdv)
        wq = jax.random.uniform(k4, (IN_DIM, OUT_DIM), dtype=jnp.float32, minval=-stdv, maxval=stdv)
        wk = jax.random.uniform(k5, (IN_DIM, OUT_DIM), dtype=jnp.float32, minval=-stdv, maxval=stdv)
        return {'feature': feature, 'graph': graph, 'weight': weight, 'wq': wq, 'wk': wk}
    _L0_gnn_all = _L0_gnn_setup()
    _L0_gnn_in = {k: v for k, v in _L0_gnn_all.items() if k in ('weight', 'wq', 'wk')}
    del _L0_gnn_all
    return {'x': x, 'adj': adj, 'L0_gnn_weight': _L0_gnn_in['weight'], 'L0_gnn_wq': _L0_gnn_in['wq'], 'L0_gnn_wk': _L0_gnn_in['wk']}

def reference(x, adj, L0_gnn_weight, L0_gnn_wq, L0_gnn_wk):
    import jax
    import jax.numpy as jnp

    def _L0_gnn_ref(feature, graph, weight, wq, wk):
        import jax, jax.numpy as jnp
        import numpy as np
        IN_DIM = 512
        OUT_DIM = 512
        BATCH = 128
        NUM_OBJS = 100
        output = jnp.einsum('bni,io->bno', feature, weight)
        q = jnp.einsum('bni,io->bno', feature, wq)
        k = jnp.einsum('bni,io->bno', feature, wk)
        alpha = jnp.einsum('bno,bmo->bnm', q, k)
        alpha = jnp.maximum(alpha, 0.0) * (graph != 0).astype(alpha.dtype)
        alpha = jax.nn.softmax(alpha, axis=1)
        return jnp.einsum('bnm,bmo->bno', alpha, output)
    h = jnp.maximum(_layernorm(x, axis=-1), 0.0)
    x = x + _L0_gnn_ref(h, adj, L0_gnn_weight, L0_gnn_wq, L0_gnn_wk)
    return x

_drawn_inputs = setup_inputs


def setup_inputs(seed=0):
    import zlib

    import numpy as np

    out = dict(_drawn_inputs(seed))
    spreads = {}
    factors = {}
    for name, (base, spread) in spreads.items():
        noise = np.random.default_rng([zlib.crc32(name.encode()), seed]).standard_normal(out[name].shape)
        drawn = base * np.exp(spread * noise) if base else spread * noise
        out[name] = jnp.asarray(drawn.astype(out[name].dtype))
    for name, factor in factors.items():
        out[name] = (out[name] * factor).astype(out[name].dtype)
    return out
```

```python
import concourse.bass as bass
from concourse import mybir
from contextlib import ExitStack


def graph_attention_kernel(nc, x, adj, weight, wq, wk, out):
    F32, F16, BF16, I32 = mybir.dt.float32, mybir.dt.float16, mybir.dt.bfloat16, mybir.dt.int32
    ALU = mybir.AluOpType
    ACT = mybir.ActivationFunctionType
    AX = mybir.AxisListType

    B, N, D = x.shape
    K = D // N
    GB = 4
    G = B // GB
    UNROLL = 4
    TURNS = (G - 2) // UNROLL
    REST = range(1 + TURNS * UNROLL, G)
    LAST = G - 1
    SCALE_STEPS = 7
    EPS = 1e-5
    MASKED = -2.0 ** 127
    P_SCALE = 2.0 ** 14
    EXP_MASK = 0x7F800000
    INV_BITS = float(0x7F000000)
    assert N == 128 and D == 512 and B % GB == 0 and TURNS > 1 and len(REST) >= 2

    def later(g):
        return not (isinstance(g, int) and g == 0)

    def use_m(k):
        return k

    def use_v(g, b):
        return 2 * K + 12 * g + b

    def use_t(g, c):
        return K + 12 * g + c if isinstance(g, int) and g == 0 else 12 * g + c

    def use_out(g, b):
        return 2 * K + 12 * g + b + (4 if isinstance(g, int) and g == LAST else 8)

    def hi_v(g, b):
        return 2 * K + 8 * g + b

    def hi_t(g, c):
        return K + c + 8 * g

    x_dram = x.rearrange("b n d -> n b d")
    adj_dram = adj.rearrange("b n m -> n b m")
    out_dram = out.rearrange("b n d -> n b d")

    ctx = ExitStack()
    with ctx:
        def sb(name, shape, dt):
            return ctx.enter_context(nc.sbuf_tensor(name, shape, dt))

        def pb(name, shape, dt):
            return ctx.enter_context(nc.psum_tensor(name, shape, dt))

        def sem(name):
            return ctx.enter_context(nc.semaphore(name))

        x_sb = sb("x_sb", [N, UNROLL, GB, D], F32)
        adj_sb = sb("adj_sb", [N, 2, GB, N], I32)
        mask = sb("mask", [N, 2, GB, N], BF16)
        h = sb("h", [N, GB, D], F32)
        hT_hi = sb("hT_hi", [N, 2, K, GB, N], F16)
        hT_lo = sb("hT_lo", [N, 2, K, GB, N], F16)
        tT_hi = sb("tT_hi", [N, K, GB, N], F16)
        tT_lo = sb("tT_lo", [N, K, GB, N], F16)
        v_hi = sb("v_hi", [N, GB, D], F16)
        v_lo = sb("v_lo", [N, GB, D], F16)
        w_sb = sb("w_sb", [N, K, D], F32)
        wq_sb = sb("wq_sb", [N, K, D], F32)
        wk_sb = sb("wk_sb", [N, K, D], F32)
        wqT = sb("wqT", [N, K, D], F32)
        wkT = sb("wkT", [N, K, D], F32)
        w_hi = sb("w_hi", [N, K, D], F16)
        w_lo = sb("w_lo", [N, K, D], F16)
        m_hi = sb("m_hi", [N, K, D], F16)
        m_lo = sb("m_lo", [N, K, D], F16)
        ident = sb("ident", [N, N], F32)
        ident_bf = sb("ident_bf", [N, N], BF16)
        w_max = sb("w_max", [N, 3], F32)
        w_top = sb("w_top", [N, 3], F32)
        w_top2 = sb("w_top2", [N, 3], F32)
        pow2 = sb("pow2", [N, 3], F32)
        ipow2 = sb("ipow2", [N, 3], F32)
        w_scale = sb("w_scale", [N, 1], F32)
        m_scale = sb("m_scale", [N, 1], F32)
        s_unscale = sb("s_unscale", [N, 1], F32)
        out_unscale = sb("out_unscale", [N, 1], F32)
        raw_stats = sb("raw_stats", [N, GB, 6], F32)
        mean_var = sb("mean_var", [N, GB, 2], F32)
        eps = sb("eps", [N, GB], F32)
        minus_one = sb("minus_one", [N, GB], F32)
        minus_half = sb("minus_half", [N, GB], F32)
        var_eps = sb("var_eps", [N, GB], F32)
        neg_mean = sb("neg_mean", [N, GB], F32)
        rstd = sb("rstd", [N, GB], F32)
        shift = sb("shift", [N, GB], F32)
        row_max = sb("row_max", [N, GB], F32)
        row_top = sb("row_top", [N, GB], F32)
        below_max = sb("below_max", [N, GB, N], F32)
        exps = sb("exps", [N, GB, N], F32)
        row_sum = sb("row_sum", [N, GB], F32)
        row_sum_s = sb("row_sum_s", [N, GB], F32)
        row_inv = sb("row_inv", [N, GB], F32)
        probs = sb("probs", [N, GB, N], F32)
        p_hi = sb("p_hi", [N, GB, N], F16)
        p_lo = sb("p_lo", [N, GB, N], F16)

        bank = [pb(f"bank{k}", [N, D], F32) for k in range(4)]
        t_bank = [pb(f"t_bank{k}", [N, K, N], F32) for k in range(2)]
        s_bank = pb("s_bank", [N, GB, N], F32)

        x_loaded = [sem(f"x_loaded{s}") for s in range(UNROLL)]
        adj_loaded = [sem(f"adj_loaded{s}") for s in range(2)]
        stored = [sem(f"stored{s}") for s in range(UNROLL)]
        w_loaded = sem("w_loaded")
        wq_loaded = sem("wq_loaded")
        wk_loaded = sem("wk_loaded")
        ident_zeroed = sem("ident_zeroed")
        consts_made = sem("consts_made")
        ident_made = sem("ident_made")
        ident_bf_made = sem("ident_bf_made")
        w_maxed = sem("w_maxed")
        w_reduced = sem("w_reduced")
        scale_step = sem("scale_step")
        w_hi_made = sem("w_hi_made")
        w_split = sem("w_split")
        wT_filled = sem("wT_filled")
        wT_copied_act = sem("wT_copied_act")
        wT_copied_vec = sem("wT_copied_vec")
        filled = sem("filled")
        hi_made = sem("hi_made")
        emptied = sem("emptied")
        stats_taken = sem("stats_taken")
        meanvar_made = sem("meanvar_made")
        ln_step = sem("ln_step")
        rstd_made = sem("rstd_made")
        h_made = sem("h_made")
        hT_filled = sem("hT_filled")
        hT_hi_made = sem("hT_hi_made")
        hT_emptied = sem("hT_emptied")
        mask_made = sem("mask_made")
        scores_filled = sem("scores_filled")
        max_found = sem("max_found")
        max_clamped = sem("max_clamped")
        scores_read = sem("scores_read")
        exp_made = sem("exp_made")
        sum_made = sem("sum_made")
        sum_scaled = sem("sum_scaled")
        inv_made = sem("inv_made")
        probs_made = sem("probs_made")
        p_split = sem("p_split")

        block = ctx.enter_context(nc.Block())

        @block.sync
        def _(sp):
            def load_x(g, s):
                sp.dma_start(x_sb[:, s], x_dram[:, bass.ds(g * GB, GB), :]).then_inc(x_loaded[s], 16)

            def load_adj(g, s):
                sp.dma_start(adj_sb[:, s], adj_dram[:, bass.ds(g * GB, GB), :]).then_inc(adj_loaded[s], 16)

            def group(i, j, more_x=True, more_adj=True):
                g = i * UNROLL + j
                if more_x:
                    sp.wait_ge(stored[(j - 1) % UNROLL], (i + (j > 0)) * (16 * GB))
                    load_x(g + UNROLL - 1, (j - 1) % UNROLL)
                if more_adj:
                    sp.wait_ge(mask_made, g + 1)
                    load_adj(g + 2, j % 2)
                for b in range(GB):
                    sp.wait_ge(emptied, use_out(g, b) + 1)
                    sp.dma_start(out_dram[:, bass.ds(g * GB + b, 1), :], x_sb[:, j, b:b + 1]).then_inc(stored[j], 16)

            sp.dma_start(wq_sb[:], wq.rearrange("(k p) d -> p k d", p=N)).then_inc(wq_loaded, 16)
            load_x(0, 0)
            load_x(1, 1)
            load_adj(0, 0)
            load_adj(1, 1)
            load_x(2, 2)
            load_x(3, 3)
            group(0, 0, more_x=False)
            with sp.Fori(0, TURNS) as i:
                for j in range(1, UNROLL + 1):
                    group(i + j // UNROLL, j % UNROLL)
            for g in REST:
                group(g // UNROLL, g % UNROLL, more_x=False, more_adj=g + 2 < G)
            for s in range(UNROLL):
                sp.wait_ge(stored[s], 16 * B // UNROLL)

        @block.gpsimd
        def _(pool):
            nc.gpsimd.memset(ident[:], 0.0).then_inc(ident_zeroed, 1)
            nc.gpsimd.memset(ident_bf[:], 0.0).then_inc(ident_zeroed, 1)
            nc.gpsimd.memset(eps[:], EPS).then_inc(consts_made, 1)
            nc.gpsimd.memset(minus_one[:], -1.0).then_inc(consts_made, 1)
            nc.gpsimd.memset(minus_half[:], -0.5).then_inc(consts_made, 1)
            pool.wait_ge(ident_zeroed, 2)
            for t, s in ((ident, ident_made), (ident_bf, ident_bf_made)):
                nc.gpsimd.affine_select(out=t[:], in_=t[:], compare_op=ALU.not_equal, fill=1.0, base=0,
                                        pattern=[[-1, N]], channel_multiplier=1).then_inc(s, 1)

            def layernorm_scales(g):
                pool.wait_ge(meanvar_made, GB * g + GB)
                if later(g):
                    pool.wait_ge(h_made, GB * g)
                nc.gpsimd.tensor_tensor(var_eps[:], mean_var[:, :, 1], eps[:], ALU.add).then_inc(ln_step, 1)
                nc.gpsimd.tensor_tensor(neg_mean[:], mean_var[:, :, 0], minus_one[:], ALU.mult).then_inc(ln_step, 1)
                pool.wait_ge(ln_step, 3 * g + 2)
                nc.gpsimd.tensor_tensor(rstd[:], var_eps[:], minus_half[:], ALU.pow).then_inc(ln_step, 1)
                pool.wait_ge(ln_step, 3 * g + 3)
                nc.gpsimd.tensor_tensor(shift[:], neg_mean[:], rstd[:], ALU.mult).then_inc(rstd_made, 1)

            def normalise(g):
                inv = row_inv[:].unsqueeze(2).to_broadcast([N, GB, N])
                pool.wait_ge(inv_made, g + 1)
                nc.gpsimd.tensor_tensor(probs[:], exps[:], inv, ALU.mult).then_inc(probs_made, 1)
                if later(g):
                    pool.wait_ge(filled, use_out(g - 1, GB - 1) + 1)
                nc.gpsimd.tensor_tensor(p_hi[:], exps[:], inv, ALU.mult).then_inc(probs_made, 1)
                pool.wait_ge(probs_made, 2 * g + 2)
                nc.gpsimd.tensor_tensor(p_lo[:], probs[:], p_hi[:], ALU.subtract).then_inc(p_split, 1)

            pool.wait_ge(consts_made, 3)
            layernorm_scales(0)
            pool.wait_ge(w_maxed, 3)
            nc.gpsimd.partition_all_reduce(w_top[:], w_max[:], N, bass.bass_isa.ReduceOp.max).then_inc(w_reduced, 1)
            layernorm_scales(1)
            layernorm_scales(2)
            normalise(0)
            with pool.Fori(0, TURNS) as i:
                for j in range(1, UNROLL + 1):
                    layernorm_scales(i * UNROLL + j + 2)
                    normalise(i * UNROLL + j)
            for g in REST:
                if g + 2 < G:
                    layernorm_scales(g + 2)
                normalise(g)

        @block.scalar
        def _(act):
            act.dma_start(wk_sb[:], wk.rearrange("(k p) d -> p k d", p=N)).then_inc(wk_loaded, 16)
            act.dma_start(w_sb[:], weight.rearrange("(k p) d -> p k d", p=N)).then_inc(w_loaded, 16)

            def normalise_h(g, s, b):
                act.wait_ge(rstd_made, g + 1)
                if later(g):
                    act.wait_ge(hT_filled, GB * (g - 1) + b + 1)
                nc.scalar.activation(h[:, b], x_sb[:, s, b], ACT.Relu, bias=shift[:, b:b + 1],
                                     scale=rstd[:, b:b + 1]).then_inc(h_made, 1)

            def hi_of_hT(g, j, b):
                act.wait_ge(hT_filled, GB * g + b + 1)
                nc.scalar.activation(hT_hi[:, j % 2, :, b, :], t_bank[b % 2][:], ACT.Copy).then_inc(hT_hi_made, 1)

            def hi_of_v(g, b):
                act.wait_ge(filled, use_v(g, b) + 1)
                nc.scalar.activation(v_hi[:, b], bank[b][:], ACT.Copy).then_inc(hi_made, 1)

            def hi_of_t(g, c):
                act.wait_ge(filled, use_t(g, c) + 1)
                nc.scalar.activation(tT_hi[:, c], bank[c][:].rearrange("p (b n) -> p b n", b=GB),
                                     ACT.Copy).then_inc(hi_made, 1)

            def exponentials(g):
                act.wait_ge(scores_read, g + 1)
                if later(g):
                    act.wait_ge(p_split, g)
                nc.scalar.activation(exps[:], below_max[:], ACT.Exp, scale=s_unscale[:]).then_inc(exp_made, 1)

            def group(i, j, nxt=True, nxt2=True):
                g = i * UNROLL + j
                for b in range(GB):
                    hi_of_v(g, b)
                if nxt2:
                    normalise_h(g + 2, (j + 2) % UNROLL, 0)
                    normalise_h(g + 2, (j + 2) % UNROLL, 1)
                exponentials(g)
                for c in range(K):
                    if nxt:
                        hi_of_t(g + 1, c)
                    if nxt2:
                        hi_of_hT(g + 2, j, c)
                        if c < 2:
                            normalise_h(g + 2, (j + 2) % UNROLL, c + 2)

            for b in range(GB):
                normalise_h(0, 0, b)
            for k in range(K):
                act.wait_ge(wT_filled, k + 1)
                nc.scalar.activation(wqT[:, k], bank[k][:], ACT.Copy).then_inc(wT_copied_act, 1)
            for b in range(GB):
                hi_of_hT(0, 0, b)
            act.wait_ge(scale_step, SCALE_STEPS)
            for k in range(K):
                act.wait_ge(filled, use_m(k) + 1)
                nc.scalar.activation(m_hi[:, k], bank[k][:], ACT.Copy, scale=m_scale[:]).then_inc(hi_made, 1)
            nc.scalar.activation(w_hi[:], w_sb[:], ACT.Copy, scale=w_scale[:]).then_inc(w_hi_made, 1)
            for b in range(GB):
                normalise_h(1, 1, b)
            for c in range(K):
                hi_of_t(0, c)
                hi_of_hT(1, 1, c)

            group(0, 0)
            with act.Fori(0, TURNS) as i:
                for j in range(1, UNROLL + 1):
                    group(i + j // UNROLL, j % UNROLL)
            for g in REST:
                group(g // UNROLL, g % UNROLL, nxt=g + 1 < G, nxt2=g + 2 < G)

        @block.vector
        def _(vec):
            def stats(g, s, loads, b):
                if b == 0:
                    vec.wait_ge(x_loaded[s], 16 * loads)
                    if later(g):
                        vec.wait_ge(rstd_made, g)
                nc.vector.bn_stats(raw_stats[:, b], x_sb[:, s, b]).then_inc(stats_taken, 1)

            def mean_variance(g, b):
                nc.vector.bn_aggr(mean_var[:, b], raw_stats[:, b]).then_inc(meanvar_made, 1)

            def lo_of_hT(g, j, b):
                vec.wait_ge(hT_hi_made, GB * g + b + 1)
                nc.vector.tensor_tensor(hT_lo[:, j % 2, :, b, :], t_bank[b % 2][:], hT_hi[:, j % 2, :, b, :],
                                        ALU.subtract).then_inc(hT_emptied, 1)

            def lo_of_v(g, b):
                vec.wait_ge(hi_made, hi_v(g, b) + 1)
                nc.vector.tensor_tensor(v_lo[:, b], bank[b][:], v_hi[:, b], ALU.subtract).then_inc(emptied, 1)

            def lo_of_t(g, c):
                vec.wait_ge(hi_made, hi_t(g, c) + 1)
                nc.vector.tensor_tensor(tT_lo[:, c], bank[c][:].rearrange("p (b n) -> p b n", b=GB), tT_hi[:, c],
                                        ALU.subtract).then_inc(emptied, 1)

            def make_mask(g, s, loads):
                vec.wait_ge(adj_loaded[s], 16 * loads)
                if later(g):
                    vec.wait_ge(scores_filled, g - 1)
                nc.vector.tensor_scalar(mask[:, s], adj_sb[:, s], 0.0, MASKED, ALU.is_equal,
                                        ALU.mult).then_inc(mask_made, 1)

            def softmax_shift(g):
                vec.wait_ge(scores_filled, g + 1)
                nc.vector.tensor_reduce(row_max[:], s_bank[:], AX.X, ALU.max).then_inc(max_found, 1)
                vec.wait_ge(max_found, g + 1)
                nc.vector.tensor_scalar(row_top[:], row_max[:], 0.0, None, ALU.max).then_inc(max_clamped, 1)
                vec.wait_ge(max_clamped, g + 1)
                nc.vector.scalar_tensor_tensor(below_max[:], s_bank[:], 0.0,
                                               row_top[:].unsqueeze(2).to_broadcast([N, GB, N]),
                                               ALU.max, ALU.subtract).then_inc(scores_read, 1)

            def softmax_sum(g):
                vec.wait_ge(exp_made, g + 1)
                nc.vector.tensor_reduce(row_sum[:], exps[:], AX.X, ALU.add).then_inc(sum_made, 1)
                vec.wait_ge(sum_made, g + 1)
                nc.vector.tensor_scalar(row_sum_s[:], row_sum[:], 1.0 / P_SCALE, None,
                                        ALU.mult).then_inc(sum_scaled, 1)
                vec.wait_ge(sum_scaled, g + 1)
                if later(g):
                    vec.wait_ge(probs_made, 2 * g)
                nc.vector.reciprocal(row_inv[:], row_sum_s[:]).then_inc(inv_made, 1)

            def residual(g, j, b):
                vec.wait_ge(filled, use_out(g, b) + 1)
                nc.vector.scalar_tensor_tensor(x_sb[:, j, b], bank[b][:], out_unscale[:], x_sb[:, j, b],
                                               ALU.mult, ALU.add).then_inc(emptied, 1)

            def group(i, j, nxt=True, nxt2=True):
                g = i * UNROLL + j
                for b in range(GB):
                    if nxt2 and b > 0:
                        vec.wait_ge(stats_taken, GB * (g + 2) + b)
                    lo_of_v(g, b)
                    if nxt2:
                        if b > 0:
                            mean_variance(g + 2, b - 1)
                        stats(g + 2, (j + 2) % UNROLL, i + (j + 2) // UNROLL + 1, b)
                if nxt:
                    if nxt2:
                        vec.wait_ge(stats_taken, GB * (g + 2) + GB)
                    make_mask(g + 1, (j + 1) % 2, i * (UNROLL // 2) + (j + 1) // 2 + 1)
                    if nxt2:
                        mean_variance(g + 2, GB - 1)
                softmax_shift(g)
                for c in range(K):
                    if nxt:
                        lo_of_t(g + 1, c)
                    if nxt2:
                        lo_of_hT(g + 2, j, c)
                    if c == 0:
                        softmax_sum(g)
                for b in range(GB):
                    residual(g, j, b)

            for b in range(GB):
                stats(0, 0, 1, b)
                vec.wait_ge(stats_taken, b + 1)
                mean_variance(0, b)
            for w, loaded, col in ((wq_sb, wq_loaded, 1), (wk_sb, wk_loaded, 2), (w_sb, w_loaded, 0)):
                if col == 0:
                    for k in range(K):
                        vec.wait_ge(wT_filled, K + k + 1)
                        nc.vector.tensor_copy(wkT[:, k], bank[k][:]).then_inc(wT_copied_vec, 1)
                vec.wait_ge(loaded, 16)
                nc.vector.tensor_reduce(w_max[:, col:col + 1], w[:].rearrange("p k d -> p (k d)"), AX.X, ALU.max,
                                        apply_absolute_value=True).then_inc(w_maxed, 1)
            for b in range(GB):
                lo_of_hT(0, 0, b)
            vec.wait_ge(w_reduced, 1)
            nc.vector.tensor_scalar(w_top2[:], w_top[:], 2.0 ** -60, 2.0 ** 60, ALU.max,
                                    ALU.min).then_inc(scale_step, 1)
            vec.wait_ge(scale_step, 1)
            nc.vector.tensor_scalar(pow2[:].bitcast(I32), w_top2[:].bitcast(I32), EXP_MASK, None,
                                    ALU.bitwise_and).then_inc(scale_step, 1)
            vec.wait_ge(scale_step, 2)
            nc.vector.tensor_scalar(ipow2[:].bitcast(I32), pow2[:].bitcast(I32), -1.0, INV_BITS, ALU.mult,
                                    ALU.add).then_inc(scale_step, 1)
            vec.wait_ge(scale_step, 3)
            nc.vector.tensor_scalar(w_scale[:], ipow2[:, 0:1], 32.0, None, ALU.mult).then_inc(scale_step, 1)
            nc.vector.scalar_tensor_tensor(m_scale[:], ipow2[:, 1:2], 16.0 / D, ipow2[:, 2:3], ALU.mult,
                                           ALU.mult).then_inc(scale_step, 1)
            nc.vector.tensor_scalar(out_unscale[:], pow2[:, 0:1], 1.0 / (32.0 * P_SCALE), None,
                                    ALU.mult).then_inc(scale_step, 1)
            nc.vector.scalar_tensor_tensor(s_unscale[:], pow2[:, 1:2], D / 16.0, pow2[:, 2:3], ALU.mult,
                                           ALU.mult).then_inc(scale_step, 1)
            vec.wait_ge(scale_step, SCALE_STEPS)
            for b in range(GB):
                stats(1, 1, 1, b)
                vec.wait_ge(stats_taken, GB + b + 1)
                mean_variance(1, b)
            for k in range(K):
                vec.wait_ge(hi_made, k + 1)
                nc.vector.scalar_tensor_tensor(m_lo[:, k], bank[k][:], m_scale[:], m_hi[:, k], ALU.mult,
                                               ALU.subtract).then_inc(emptied, 1)
            make_mask(0, 0, 1)
            for c in range(K):
                lo_of_t(0, c)
                lo_of_hT(1, 1, c)
                if c == 0:
                    vec.wait_ge(w_hi_made, 1)
                    nc.vector.scalar_tensor_tensor(w_lo[:], w_sb[:], w_scale[:], w_hi[:], ALU.mult,
                                                   ALU.subtract).then_inc(w_split, 1)

            group(0, 0)
            with vec.Fori(0, TURNS) as i:
                for j in range(1, UNROLL + 1):
                    group(i + j // UNROLL, j % UNROLL)
            for g in REST:
                group(g // UNROLL, g % UNROLL, nxt=g + 1 < G, nxt2=g + 2 < G)

        @block.tensor
        def _(pe):
            def transpose_h(g, b, n):
                pe.wait_ge(h_made, GB * g + b + 1)
                if n is not None:
                    pe.wait_ge(hT_emptied, n - 1)
                for k in range(K):
                    last = nc.tensor.transpose(t_bank[b % 2][:, k], h[:, b, k * N:(k + 1) * N], ident[:])
                last.then_inc(hT_filled, 1)

            def product_t(g, s, c):
                pe.wait_ge(emptied, use_t(g, c) - 3)
                for k in range(K):
                    mh = m_hi[:, k, c * N:(c + 1) * N]
                    ml = m_lo[:, k, c * N:(c + 1) * N]
                    nc.tensor.matmul(bank[c][:], mh, hT_hi[:, s, k], start=k == 0, stop=False)
                    nc.tensor.matmul(bank[c][:], mh, hT_lo[:, s, k], start=False, stop=False)
                    last = nc.tensor.matmul(bank[c][:], ml, hT_hi[:, s, k], start=False, stop=k == K - 1)
                last.then_inc(filled, 1)

            def product_v(g, s, b):
                pe.wait_ge(emptied, use_v(g, b) - 3)
                for k in range(K):
                    nc.tensor.matmul(bank[b][:], hT_hi[:, s, k, b], w_hi[:, k], start=k == 0, stop=False)
                    nc.tensor.matmul(bank[b][:], hT_hi[:, s, k, b], w_lo[:, k], start=False, stop=False)
                    last = nc.tensor.matmul(bank[b][:], hT_lo[:, s, k, b], w_hi[:, k], start=False, stop=k == K - 1)
                last.then_inc(filled, 1)

            def scores(g, s):
                pe.wait_ge(mask_made, g + 1)
                if later(g):
                    pe.wait_ge(scores_read, g)
                for b in range(GB):
                    o = s_bank[:, b]
                    nc.tensor.matmul(o, mask[:, s, b], ident_bf[:], start=True, stop=False)
                    for k in range(K):
                        nc.tensor.matmul(o, hT_hi[:, s, k, b], tT_hi[:, k, b], start=False, stop=False)
                        nc.tensor.matmul(o, hT_hi[:, s, k, b], tT_lo[:, k, b], start=False, stop=False)
                        last = nc.tensor.matmul(o, hT_lo[:, s, k, b], tT_hi[:, k, b], start=False, stop=k == K - 1)
                last.then_inc(scores_filled, 1)

            def product_out(g, b):
                if b == 0:
                    pe.wait_ge(p_split, g + 1)
                pe.wait_ge(emptied, use_out(g, b) - 3)
                nc.tensor.matmul(bank[b][:], p_hi[:, b], v_hi[:, b], start=True, stop=False)
                nc.tensor.matmul(bank[b][:], p_hi[:, b], v_lo[:, b], start=False, stop=False)
                nc.tensor.matmul(bank[b][:], p_lo[:, b], v_hi[:, b], start=False, stop=True).then_inc(filled, 1)

            def group(i, j, nxt=True, nxt2=True):
                g = i * UNROLL + j
                for b in range(GB):
                    product_v(g, j % 2, b)
                scores(g, j % 2)
                if nxt:
                    pe.wait_ge(hT_emptied, GB * g + 2 * GB)
                for c in range(K):
                    if nxt:
                        product_t(g + 1, (j + 1) % 2, c)
                    if nxt2:
                        transpose_h(g + 2, c, GB * (g + 2) + c)
                for b in range(GB):
                    product_out(g, b)

            pe.wait_ge(ident_made, 1)
            pe.wait_ge(wq_loaded, 16)
            for k in range(K):
                for r in range(K):
                    last = nc.tensor.transpose(bank[k][:, r * N:(r + 1) * N], wq_sb[:, r, k * N:(k + 1) * N], ident[:])
                last.then_inc(wT_filled, 1)
            pe.wait_ge(wk_loaded, 16)
            for k in range(K):
                pe.wait_ge(wT_copied_act, k + 1)
                for r in range(K):
                    last = nc.tensor.transpose(bank[k][:, r * N:(r + 1) * N], wk_sb[:, r, k * N:(k + 1) * N], ident[:])
                last.then_inc(wT_filled, 1)
            for b in range(GB):
                transpose_h(0, b, b if b >= 2 else None)
            pe.wait_ge(wT_copied_vec, K)
            for c in range(K):
                for k in range(K):
                    last = nc.tensor.matmul(bank[c][:], wqT[:, k, c * N:(c + 1) * N], wkT[:, k], start=k == 0,
                                            stop=k == K - 1)
                last.then_inc(filled, 1)
            pe.wait_ge(emptied, K)
            pe.wait_ge(hT_emptied, GB)
            for c in range(K):
                product_t(0, 0, c)
                transpose_h(1, c, GB + c)
            pe.wait_ge(w_split, 1)
            pe.wait_ge(ident_bf_made, 1)
            group(0, 0)
            with pe.Fori(0, TURNS) as i:
                for j in range(1, UNROLL + 1):
                    group(i + j // UNROLL, j % UNROLL)
            for g in REST:
                group(g // UNROLL, g % UNROLL, nxt=g + 1 < G, nxt2=g + 2 < G)


_INS = ["x", "adj", "L0_gnn_weight", "L0_gnn_wq", "L0_gnn_wk"]


def kernel(**inputs):
    import numpy as _np
    import concourse.bacc as _bacc
    from concourse import mybir as _mybir
    from concourse.bass_utils import run_bass_kernel_spmd as _run

    nc = _bacc.Bacc("TRN2", target_bir_lowering=False, num_devices=1)
    arrays, args = {}, []
    for name in _INS:
        a = _np.ascontiguousarray(inputs[name])
        arrays[f"in_{name}"] = a
        args.append(nc.dram_tensor(f"in_{name}", a.shape, _mybir.dt.from_np(a.dtype), kind="ExternalInput").ap())
    shape = inputs["x"].shape
    args.append(nc.dram_tensor("out_h", shape, _mybir.dt.float32, kind="ExternalOutput").ap())
    graph_attention_kernel(nc, *args)
    r = _run(nc, [arrays], core_ids=[0])
    return r.results[0]["out_h"]
```

```python
import concourse.bass as bass
from concourse import mybir
from contextlib import ExitStack


def graph_attention_kernel(nc, x, adj, weight, wq, wk, out):
    F32, F16, BF16, I32 = mybir.dt.float32, mybir.dt.float16, mybir.dt.bfloat16, mybir.dt.int32
    ALU = mybir.AluOpType
    ACT = mybir.ActivationFunctionType
    AX = mybir.AxisListType

    B, N, D = x.shape
    K = D // N
    GB = 4
    G = B // GB
    UNROLL = 4
    TURNS = (G - 2) // UNROLL
    REST = range(1 + TURNS * UNROLL, G)
    LAST = G - 1
    SCALE_STEPS = 8
    EPS = 1e-5
    MASKED = -2.0 ** 127
    H_SCALE = 2.0 ** 10
    W_TOP = 2.0 ** 15
    T_SCALE = 2.0 ** 15 / (H_SCALE * D * W_TOP)
    P_SCALE = 2.0 ** 14
    EXP_MASK = 0x7F800000
    INV_BITS = float(0x7F000000)
    assert N == 128 and D == 512 and B % GB == 0 and TURNS > 1 and len(REST) >= 2

    def later(g):
        return not (isinstance(g, int) and g == 0)

    def use_m(k):
        return k

    def use_v(g, b):
        return (8 + 12 * g if later(g) else K) + b

    def use_t(g, c):
        return (12 * g if later(g) else 2 * K) + c

    def use_out(g, b):
        return 12 * g + b + (12 if isinstance(g, int) and g == LAST else 16)

    def hi_v(g, b):
        return (8 + 8 * g if later(g) else K) + b

    def hi_t(g, c):
        return (4 + 8 * g if later(g) else 2 * K) + c

    x_dram = x.rearrange("b n d -> n b d")
    adj_dram = adj.rearrange("b n m -> n b m")
    out_dram = out.rearrange("b n d -> n b d")

    ctx = ExitStack()
    with ctx:
        def sb(name, shape, dt):
            return ctx.enter_context(nc.sbuf_tensor(name, shape, dt))

        def pb(name, shape, dt):
            return ctx.enter_context(nc.psum_tensor(name, shape, dt))

        def sem(name):
            return ctx.enter_context(nc.semaphore(name))

        x_sb = sb("x_sb", [N, UNROLL, GB, D], F32)
        adj_sb = sb("adj_sb", [N, 2, GB, N], I32)
        mask = sb("mask", [N, 2, GB, N], BF16)
        h = sb("h", [N, GB, D], F32)
        hT_hi = sb("hT_hi", [N, 2, K, GB, N], F16)
        hT_lo = sb("hT_lo", [N, 2, K, GB, N], F16)
        tT_hi = sb("tT_hi", [N, K, GB, N], F16)
        tT_lo = sb("tT_lo", [N, K, GB, N], F16)
        v_hi = sb("v_hi", [N, GB, D], F16)
        v_lo = sb("v_lo", [N, GB, D], F16)
        w_sb = sb("w_sb", [N, K, D], F32)
        wq_sb = sb("wq_sb", [N, K, D], F32)
        wk_sb = sb("wk_sb", [N, K, D], F32)
        wqT = sb("wqT", [N, K, K, N], F32)
        wkT = sb("wkT", [N, K, K, N], F32)
        w_hi = sb("w_hi", [N, K, D], F16)
        w_lo = sb("w_lo", [N, K, D], F16)
        m_hi = sb("m_hi", [N, K, D], F16)
        m_lo = sb("m_lo", [N, K, D], F16)
        ident = sb("ident", [N, N], F32)
        ident_bf = sb("ident_bf", [N, N], BF16)
        w_max = sb("w_max", [N, 3, K], F32)
        w_maxs = sb("w_maxs", [N, 3, K], F32)
        w_top = sb("w_top", [N, 3], F32)
        w_top2 = sb("w_top2", [N, 3], F32)
        pow2 = sb("pow2", [N, 3], F32)
        ipow2 = sb("ipow2", [N, 3], F32)
        w_scale = sb("w_scale", [N, 1], F32)
        m_scale = sb("m_scale", [N, 1], F32)
        s_unscale = sb("s_unscale", [N, 1], F32)
        out_unscale = sb("out_unscale", [N, 1], F32)
        raw_stats = sb("raw_stats", [N, GB, 6], F32)
        mean_var = sb("mean_var", [N, GB, 2], F32)
        eps = sb("eps", [N, GB], F32)
        minus_one = sb("minus_one", [N, GB], F32)
        minus_half = sb("minus_half", [N, GB], F32)
        h_scale = sb("h_scale", [N, GB], F32)
        inv_std = sb("inv_std", [N, GB], F32)
        var_eps = sb("var_eps", [N, GB], F32)
        neg_mean = sb("neg_mean", [N, GB], F32)
        rstd = sb("rstd", [N, GB], F32)
        shift = sb("shift", [N, GB], F32)
        row_max = sb("row_max", [N, GB], F32)
        row_top = sb("row_top", [N, GB], F32)
        below_max = sb("below_max", [N, GB, N], F32)
        exps = sb("exps", [N, GB, N], F32)
        row_sum = sb("row_sum", [N, GB], F32)
        row_sum_s = sb("row_sum_s", [N, GB], F32)
        row_inv = sb("row_inv", [N, GB], F32)
        probs = sb("probs", [N, GB, N], F32)
        p_hi = sb("p_hi", [N, GB, N], F16)
        p_lo = sb("p_lo", [N, GB, N], F16)

        bank = [pb(f"bank{k}", [N, D], F32) for k in range(4)]
        t_bank = [pb(f"t_bank{k}", [N, K, N], F32) for k in range(2)]
        s_bank = pb("s_bank", [N, GB, N], F32)
        start_bank = [t_bank[0], t_bank[1], s_bank, pb("spare_bank", [N, K, N], F32)]

        x_loaded = [sem(f"x_loaded{s}") for s in range(UNROLL)]
        adj_loaded = [sem(f"adj_loaded{s}") for s in range(2)]
        stored = [sem(f"stored{s}") for s in range(UNROLL)]
        w_loaded = sem("w_loaded")
        wq_loaded = [sem(f"wq_loaded{r}") for r in range(K)]
        wk_loaded = [sem(f"wk_loaded{r}") for r in range(K)]
        ident_zeroed = sem("ident_zeroed")
        consts_made = sem("consts_made")
        ident_made = sem("ident_made")
        ident_bf_made = sem("ident_bf_made")
        w_maxed = sem("w_maxed")
        w_reduced = sem("w_reduced")
        scale_step = sem("scale_step")
        w_hi_made = sem("w_hi_made")
        w_split = sem("w_split")
        wT_filled = sem("wT_filled")
        wT_copied_act = sem("wT_copied_act")
        wT_copied_vec = sem("wT_copied_vec")
        filled = sem("filled")
        hi_made = sem("hi_made")
        emptied = sem("emptied")
        stats_taken = sem("stats_taken")
        meanvar_made = sem("meanvar_made")
        ln_step = sem("ln_step")
        rstd_made = sem("rstd_made")
        h_made = sem("h_made")
        hT_filled = sem("hT_filled")
        hT_hi_made = sem("hT_hi_made")
        hT_emptied = sem("hT_emptied")
        mask_made = sem("mask_made")
        scores_filled = sem("scores_filled")
        max_found = sem("max_found")
        max_clamped = sem("max_clamped")
        scores_read = sem("scores_read")
        exp_made = sem("exp_made")
        sum_made = sem("sum_made")
        sum_scaled = sem("sum_scaled")
        inv_made = sem("inv_made")
        probs_made = sem("probs_made")
        p_split = sem("p_split")

        block = ctx.enter_context(nc.Block())

        @block.sync
        def _(sp):
            def load_x(g, s):
                sp.dma_start(x_sb[:, s], x_dram[:, bass.ds(g * GB, GB), :]).then_inc(x_loaded[s], 16)

            def load_adj(g, s):
                sp.dma_start(adj_sb[:, s], adj_dram[:, bass.ds(g * GB, GB), :]).then_inc(adj_loaded[s], 16)

            def group(i, j, more_x=True, more_adj=True):
                g = i * UNROLL + j
                if more_x:
                    sp.wait_ge(stored[(j - 1) % UNROLL], (i + (j > 0)) * (16 * GB))
                    load_x(g + UNROLL - 1, (j - 1) % UNROLL)
                if more_adj:
                    sp.wait_ge(mask_made, g + 1)
                    load_adj(g + 2, j % 2)
                for b in range(GB):
                    sp.wait_ge(emptied, use_out(g, b) + 1)
                    sp.dma_start(out_dram[:, bass.ds(g * GB + b, 1), :], x_sb[:, j, b:b + 1]).then_inc(stored[j], 16)

            for r in range(K):
                sp.dma_start(wq_sb[:, r], wq[r * N:(r + 1) * N, :]).then_inc(wq_loaded[r], 16)
            load_x(0, 0)
            sp.dma_start(w_sb[:], weight.rearrange("(k p) d -> p k d", p=N)).then_inc(w_loaded, 16)
            load_adj(0, 0)
            load_x(1, 1)
            load_adj(1, 1)
            load_x(2, 2)
            load_x(3, 3)
            group(0, 0, more_x=False)
            with sp.Fori(0, TURNS) as i:
                for j in range(1, UNROLL + 1):
                    group(i + j // UNROLL, j % UNROLL)
            for g in REST:
                group(g // UNROLL, g % UNROLL, more_x=False, more_adj=g + 2 < G)
            for s in range(UNROLL):
                sp.wait_ge(stored[s], 16 * B // UNROLL)

        @block.gpsimd
        def _(pool):
            nc.gpsimd.memset(ident[:], 0.0).then_inc(ident_zeroed, 1)
            nc.gpsimd.memset(ident_bf[:], 0.0).then_inc(ident_zeroed, 1)
            nc.gpsimd.memset(eps[:], EPS).then_inc(consts_made, 1)
            nc.gpsimd.memset(minus_one[:], -1.0).then_inc(consts_made, 1)
            nc.gpsimd.memset(minus_half[:], -0.5).then_inc(consts_made, 1)
            nc.gpsimd.memset(h_scale[:], H_SCALE).then_inc(consts_made, 1)
            pool.wait_ge(ident_zeroed, 2)
            for t, s in ((ident, ident_made), (ident_bf, ident_bf_made)):
                nc.gpsimd.affine_select(out=t[:], in_=t[:], compare_op=ALU.not_equal, fill=1.0, base=0,
                                        pattern=[[-1, N]], channel_multiplier=1).then_inc(s, 1)

            def layernorm_scales(g):
                pool.wait_ge(meanvar_made, GB * g + GB)
                if later(g):
                    pool.wait_ge(h_made, GB * g)
                nc.gpsimd.tensor_tensor(var_eps[:], mean_var[:, :, 1], eps[:], ALU.add).then_inc(ln_step, 1)
                nc.gpsimd.tensor_tensor(neg_mean[:], mean_var[:, :, 0], minus_one[:], ALU.mult).then_inc(ln_step, 1)
                pool.wait_ge(ln_step, 4 * g + 2)
                nc.gpsimd.tensor_tensor(inv_std[:], var_eps[:], minus_half[:], ALU.pow).then_inc(ln_step, 1)
                pool.wait_ge(ln_step, 4 * g + 3)
                nc.gpsimd.tensor_tensor(rstd[:], inv_std[:], h_scale[:], ALU.mult).then_inc(ln_step, 1)
                pool.wait_ge(ln_step, 4 * g + 4)
                nc.gpsimd.tensor_tensor(shift[:], neg_mean[:], rstd[:], ALU.mult).then_inc(rstd_made, 1)

            def normalise(g):
                inv = row_inv[:].unsqueeze(2).to_broadcast([N, GB, N])
                pool.wait_ge(inv_made, g + 1)
                nc.gpsimd.tensor_tensor(probs[:], exps[:], inv, ALU.mult).then_inc(probs_made, 1)
                if later(g):
                    pool.wait_ge(filled, use_out(g - 1, GB - 1) + 1)
                nc.gpsimd.tensor_tensor(p_hi[:], exps[:], inv, ALU.mult).then_inc(probs_made, 1)
                pool.wait_ge(probs_made, 2 * g + 2)
                nc.gpsimd.tensor_tensor(p_lo[:], probs[:], p_hi[:], ALU.subtract).then_inc(p_split, 1)

            pool.wait_ge(consts_made, 4)
            layernorm_scales(0)
            pool.wait_ge(w_maxed, 5)
            nc.gpsimd.partition_all_reduce(w_maxs[:].rearrange("p w k -> p (w k)"),
                                           w_max[:].rearrange("p w k -> p (w k)"), N,
                                           bass.bass_isa.ReduceOp.max).then_inc(w_reduced, 1)
            layernorm_scales(1)
            layernorm_scales(2)
            normalise(0)
            with pool.Fori(0, TURNS) as i:
                for j in range(1, UNROLL + 1):
                    normalise(i * UNROLL + j)
                    layernorm_scales(i * UNROLL + j + 2)
            for g in REST:
                normalise(g)
                if g + 2 < G:
                    layernorm_scales(g + 2)

        @block.scalar
        def _(act):
            for r in range(K):
                act.dma_start(wk_sb[:, r], wk[r * N:(r + 1) * N, :]).then_inc(wk_loaded[r], 16)

            def normalise_h(g, s, b):
                act.wait_ge(rstd_made, g + 1)
                if later(g):
                    act.wait_ge(hT_filled, GB * (g - 1) + b + 1)
                nc.scalar.activation(h[:, b], x_sb[:, s, b], ACT.Relu, bias=shift[:, b:b + 1],
                                     scale=rstd[:, b:b + 1]).then_inc(h_made, 1)

            def hi_of_hT(g, j, b):
                act.wait_ge(hT_filled, GB * g + b + 1)
                nc.scalar.activation(hT_hi[:, j % 2, :, b, :], t_bank[b % 2][:], ACT.Copy).then_inc(hT_hi_made, 1)

            def hi_of_v(g, b):
                act.wait_ge(filled, use_v(g, b) + 1)
                nc.scalar.activation(v_hi[:, b], bank[b][:], ACT.Copy, scale=T_SCALE).then_inc(hi_made, 1)

            def hi_of_t(g, c):
                act.wait_ge(filled, use_t(g, c) + 1)
                nc.scalar.activation(tT_hi[:, c], bank[c][:].rearrange("p (b n) -> p b n", b=GB), ACT.Copy,
                                     scale=T_SCALE).then_inc(hi_made, 1)

            def exponentials(g):
                act.wait_ge(scores_read, g + 1)
                if later(g):
                    act.wait_ge(p_split, g)
                nc.scalar.activation(exps[:], below_max[:], ACT.Exp, scale=s_unscale[:]).then_inc(exp_made, 1)

            def group(i, j, nxt=True, nxt2=True):
                g = i * UNROLL + j
                s2 = (j + 2) % UNROLL
                exponentials(g)
                for b in range(GB):
                    hi_of_v(g, b)
                    if nxt2 and b == 2:
                        normalise_h(g + 2, s2, 0)
                        normalise_h(g + 2, s2, 1)
                if nxt2:
                    normalise_h(g + 2, s2, 2)
                    normalise_h(g + 2, s2, 3)
                for c in range(K):
                    if nxt:
                        hi_of_t(g + 1, c)
                    if nxt2:
                        hi_of_hT(g + 2, j, c)

            for r in range(K):
                act.wait_ge(wT_filled, 2 * r + 1)
                nc.scalar.activation(wqT[:, :, r], bank[r][:].rearrange("p (k n) -> p k n", k=K),
                                     ACT.Copy).then_inc(wT_copied_act, 1)
            for b in range(GB):
                normalise_h(0, 0, b)
            for b in range(2):
                hi_of_hT(0, 0, b)
            act.wait_ge(scale_step, SCALE_STEPS)
            for k in range(K):
                nc.scalar.activation(w_hi[:, k], w_sb[:, k], ACT.Copy, scale=w_scale[:]).then_inc(w_hi_made, 1)
            for k in range(K):
                act.wait_ge(filled, use_m(k) + 1)
                nc.scalar.activation(m_hi[:, k], bank[k][:], ACT.Copy, scale=m_scale[:]).then_inc(hi_made, 1)
                if k < 2:
                    hi_of_hT(0, 0, k + 2)
            for b in range(2):
                hi_of_v(0, b)
            for b in range(2):
                normalise_h(1, 1, b)
                hi_of_v(0, b + 2)
            for b in range(2, GB):
                normalise_h(1, 1, b)
            for c in range(K):
                hi_of_t(0, c)
                if c < 2:
                    hi_of_hT(1, 1, c)
            hi_of_hT(1, 1, 2)
            hi_of_hT(1, 1, 3)
            normalise_h(2, 2, 0)
            exponentials(0)
            normalise_h(2, 2, 1)
            for c in range(K):
                hi_of_t(1, c)
                hi_of_hT(2, 0, c)
                if c < 2:
                    normalise_h(2, 2, c + 2)
            with act.Fori(0, TURNS) as i:
                for j in range(1, UNROLL + 1):
                    group(i + j // UNROLL, j % UNROLL)
            for g in REST:
                group(g // UNROLL, g % UNROLL, nxt=g + 1 < G, nxt2=g + 2 < G)

        @block.vector
        def _(vec):
            def stats(g, s, loads, b):
                if b == 0:
                    vec.wait_ge(x_loaded[s], 16 * loads)
                    if later(g):
                        vec.wait_ge(rstd_made, g)
                nc.vector.bn_stats(raw_stats[:, b], x_sb[:, s, b]).then_inc(stats_taken, 1)

            def mean_variance(g, b):
                nc.vector.bn_aggr(mean_var[:, b], raw_stats[:, b]).then_inc(meanvar_made, 1)

            def lo_of_hT(g, j, b):
                vec.wait_ge(hT_hi_made, GB * g + b + 1)
                nc.vector.tensor_tensor(hT_lo[:, j % 2, :, b, :], t_bank[b % 2][:], hT_hi[:, j % 2, :, b, :],
                                        ALU.subtract).then_inc(hT_emptied, 1)

            def lo_of_v(g, b):
                vec.wait_ge(hi_made, hi_v(g, b) + 1)
                nc.vector.scalar_tensor_tensor(v_lo[:, b], bank[b][:], T_SCALE, v_hi[:, b], ALU.mult,
                                               ALU.subtract).then_inc(emptied, 1)

            def lo_of_t(g, c):
                vec.wait_ge(hi_made, hi_t(g, c) + 1)
                nc.vector.scalar_tensor_tensor(tT_lo[:, c], bank[c][:].rearrange("p (b n) -> p b n", b=GB), T_SCALE,
                                               tT_hi[:, c], ALU.mult, ALU.subtract).then_inc(emptied, 1)

            def make_mask(g, s, loads):
                vec.wait_ge(adj_loaded[s], 16 * loads)
                if not isinstance(g, int) or g > 1:
                    vec.wait_ge(scores_filled, g - 1)
                nc.vector.tensor_scalar(mask[:, s], adj_sb[:, s], 0.0, MASKED, ALU.is_equal,
                                        ALU.mult).then_inc(mask_made, 1)

            def softmax_shift(g):
                vec.wait_ge(scores_filled, g + 1)
                nc.vector.tensor_reduce(row_max[:], s_bank[:], AX.X, ALU.max).then_inc(max_found, 1)
                vec.wait_ge(max_found, g + 1)
                nc.vector.tensor_scalar(row_top[:], row_max[:], 0.0, None, ALU.max).then_inc(max_clamped, 1)
                vec.wait_ge(max_clamped, g + 1)
                nc.vector.scalar_tensor_tensor(below_max[:], s_bank[:], 0.0,
                                               row_top[:].unsqueeze(2).to_broadcast([N, GB, N]),
                                               ALU.max, ALU.subtract).then_inc(scores_read, 1)

            def softmax_sum(g):
                vec.wait_ge(exp_made, g + 1)
                nc.vector.tensor_reduce(row_sum[:], exps[:], AX.X, ALU.add).then_inc(sum_made, 1)
                vec.wait_ge(sum_made, g + 1)
                nc.vector.tensor_scalar(row_sum_s[:], row_sum[:], 1.0 / P_SCALE, None,
                                        ALU.mult).then_inc(sum_scaled, 1)
                vec.wait_ge(sum_scaled, g + 1)
                if later(g):
                    vec.wait_ge(probs_made, 2 * g)
                nc.vector.reciprocal(row_inv[:], row_sum_s[:]).then_inc(inv_made, 1)

            def residual(g, j, b):
                vec.wait_ge(filled, use_out(g, b) + 1)
                nc.vector.scalar_tensor_tensor(x_sb[:, j, b], bank[b][:], out_unscale[:], x_sb[:, j, b],
                                               ALU.mult, ALU.add).then_inc(emptied, 1)

            def group(i, j, nxt=True, nxt2=True):
                g = i * UNROLL + j

                def stats2(b):
                    stats(g + 2, (j + 2) % UNROLL, i + (j + 2) // UNROLL + 1, b)

                if nxt2:
                    stats2(0)
                    vec.wait_ge(stats_taken, GB * (g + 2) + 1)
                if nxt:
                    make_mask(g + 1, (j + 1) % 2, i * (UNROLL // 2) + (j + 1) // 2 + 1)
                if nxt2:
                    mean_variance(g + 2, 0)
                softmax_shift(g)
                if nxt2:
                    stats2(1)
                    vec.wait_ge(stats_taken, GB * (g + 2) + 2)
                lo_of_v(g, 0)
                if nxt2:
                    mean_variance(g + 2, 1)
                softmax_sum(g)
                if nxt2:
                    stats2(2)
                    stats2(3)
                    vec.wait_ge(stats_taken, GB * (g + 2) + 4)
                lo_of_v(g, 1)
                if nxt2:
                    mean_variance(g + 2, 2)
                    mean_variance(g + 2, 3)
                lo_of_v(g, 2)
                lo_of_v(g, 3)
                for c in range(K):
                    if nxt:
                        lo_of_t(g + 1, c)
                    if nxt2:
                        lo_of_hT(g + 2, j, c)
                for b in range(GB):
                    residual(g, j, b)

            def stats_all(g, s, b):
                stats(g, s, 1, b)
                vec.wait_ge(stats_taken, GB * g + b + 1)
                mean_variance(g, b)

            def weight_max(w, out):
                nc.vector.tensor_reduce(out, w, AX.X, ALU.max, apply_absolute_value=True).then_inc(w_maxed, 1)

            for r in range(K):
                vec.wait_ge(wq_loaded[r], 16)
                if r < 2:
                    weight_max(wq_sb[:, r], w_max[:, 1, r:r + 1])
                vec.wait_ge(wT_filled, 2 * r + 2)
                nc.vector.tensor_copy(wkT[:, :, r], start_bank[r][:]).then_inc(wT_copied_vec, 1)
            weight_max(wq_sb[:, 2:], w_max[:, 1, 2:])
            for b in range(GB):
                stats_all(0, 0, b)
            for r in range(K):
                vec.wait_ge(wk_loaded[r], 16)
            weight_max(wk_sb[:], w_max[:, 2])
            vec.wait_ge(w_loaded, 16)
            weight_max(w_sb[:], w_max[:, 0])
            vec.wait_ge(w_reduced, 1)
            nc.vector.tensor_reduce(w_top[:], w_maxs[:], AX.X, ALU.max).then_inc(scale_step, 1)
            vec.wait_ge(scale_step, 1)
            nc.vector.tensor_scalar(w_top2[:], w_top[:], 2.0 ** -60, 2.0 ** 60, ALU.max,
                                    ALU.min).then_inc(scale_step, 1)
            vec.wait_ge(scale_step, 2)
            nc.vector.tensor_scalar(pow2[:].bitcast(I32), w_top2[:].bitcast(I32), EXP_MASK, None,
                                    ALU.bitwise_and).then_inc(scale_step, 1)
            vec.wait_ge(scale_step, 3)
            nc.vector.tensor_scalar(ipow2[:].bitcast(I32), pow2[:].bitcast(I32), -1.0, INV_BITS, ALU.mult,
                                    ALU.add).then_inc(scale_step, 1)
            vec.wait_ge(scale_step, 4)
            w_factor, m_factor = W_TOP / 2, W_TOP / (4 * D)
            nc.vector.tensor_scalar(w_scale[:], ipow2[:, 0:1], w_factor, None, ALU.mult).then_inc(scale_step, 1)
            nc.vector.scalar_tensor_tensor(m_scale[:], ipow2[:, 1:2], m_factor, ipow2[:, 2:3], ALU.mult,
                                           ALU.mult).then_inc(scale_step, 1)
            nc.vector.tensor_scalar(out_unscale[:], pow2[:, 0:1], 1.0 / (P_SCALE * H_SCALE * T_SCALE * w_factor), None,
                                    ALU.mult).then_inc(scale_step, 1)
            nc.vector.scalar_tensor_tensor(s_unscale[:], pow2[:, 1:2], 1.0 / (H_SCALE ** 2 * T_SCALE * m_factor),
                                           pow2[:, 2:3], ALU.mult, ALU.mult).then_inc(scale_step, 1)
            vec.wait_ge(scale_step, SCALE_STEPS)
            for b in range(2):
                lo_of_hT(0, 0, b)
            for k in range(K):
                vec.wait_ge(w_hi_made, k + 1)
                nc.vector.scalar_tensor_tensor(w_lo[:, k], w_sb[:, k], w_scale[:], w_hi[:, k], ALU.mult,
                                               ALU.subtract).then_inc(w_split, 1)
            for k in range(K):
                vec.wait_ge(hi_made, k + 1)
                nc.vector.scalar_tensor_tensor(m_lo[:, k], bank[k][:], m_scale[:], m_hi[:, k], ALU.mult,
                                               ALU.subtract).then_inc(emptied, 1)
                if k < 2:
                    lo_of_hT(0, 0, k + 2)
            make_mask(0, 0, 1)
            for b in range(GB):
                stats_all(1, 1, b)
            for b in range(GB):
                lo_of_v(0, b)
            make_mask(1, 1, 1)
            for c in range(K):
                lo_of_t(0, c)
                if c < 2:
                    lo_of_hT(1, 1, c)
                    stats_all(2, 2, c)
            lo_of_hT(1, 1, 2)
            lo_of_hT(1, 1, 3)
            stats_all(2, 2, 2)
            stats_all(2, 2, 3)
            softmax_shift(0)
            for c in range(K):
                lo_of_t(1, c)
                lo_of_hT(2, 0, c)
                if c == 0:
                    softmax_sum(0)
            for b in range(GB):
                residual(0, 0, b)
            with vec.Fori(0, TURNS) as i:
                for j in range(1, UNROLL + 1):
                    group(i + j // UNROLL, j % UNROLL)
            for g in REST:
                group(g // UNROLL, g % UNROLL, nxt=g + 1 < G, nxt2=g + 2 < G)

        @block.tensor
        def _(pe):
            def transpose_h(g, b):
                pe.wait_ge(h_made, GB * g + b + 1)
                if later(g) or b >= 2:
                    pe.wait_ge(hT_emptied, GB * g + b - 1)
                for k in range(K):
                    last = nc.tensor.transpose(t_bank[b % 2][:, k], h[:, b, k * N:(k + 1) * N], ident[:])
                last.then_inc(hT_filled, 1)

            def product_t(g, s, c):
                pe.wait_ge(emptied, use_t(g, c) - 3)
                for k in range(K):
                    mh = m_hi[:, k, c * N:(c + 1) * N]
                    ml = m_lo[:, k, c * N:(c + 1) * N]
                    nc.tensor.matmul(bank[c][:], mh, hT_hi[:, s, k], start=k == 0, stop=False)
                    nc.tensor.matmul(bank[c][:], mh, hT_lo[:, s, k], start=False, stop=False)
                    last = nc.tensor.matmul(bank[c][:], ml, hT_hi[:, s, k], start=False, stop=k == K - 1)
                last.then_inc(filled, 1)

            def product_v(g, s, b):
                pe.wait_ge(emptied, use_v(g, b) - 3)
                for k in range(K):
                    nc.tensor.matmul(bank[b][:], hT_hi[:, s, k, b], w_hi[:, k], start=k == 0, stop=False)
                    nc.tensor.matmul(bank[b][:], hT_hi[:, s, k, b], w_lo[:, k], start=False, stop=False)
                    last = nc.tensor.matmul(bank[b][:], hT_lo[:, s, k, b], w_hi[:, k], start=False, stop=k == K - 1)
                last.then_inc(filled, 1)

            def scores(g, s):
                pe.wait_ge(emptied, use_t(g, K - 1) + 1)
                pe.wait_ge(mask_made, g + 1)
                if later(g):
                    pe.wait_ge(scores_read, g)
                for b in range(GB):
                    o = s_bank[:, b]
                    nc.tensor.matmul(o, mask[:, s, b], ident_bf[:], start=True, stop=False)
                    for k in range(K):
                        nc.tensor.matmul(o, hT_hi[:, s, k, b], tT_hi[:, k, b], start=False, stop=False)
                        nc.tensor.matmul(o, hT_hi[:, s, k, b], tT_lo[:, k, b], start=False, stop=False)
                        last = nc.tensor.matmul(o, hT_lo[:, s, k, b], tT_hi[:, k, b], start=False, stop=k == K - 1)
                last.then_inc(scores_filled, 1)

            def product_out(g, b):
                if b == 0:
                    pe.wait_ge(p_split, g + 1)
                pe.wait_ge(emptied, use_out(g, b) - 3)
                nc.tensor.matmul(bank[b][:], p_hi[:, b], v_hi[:, b], start=True, stop=False)
                nc.tensor.matmul(bank[b][:], p_hi[:, b], v_lo[:, b], start=False, stop=False)
                nc.tensor.matmul(bank[b][:], p_lo[:, b], v_hi[:, b], start=False, stop=True).then_inc(filled, 1)

            def group(i, j, nxt=True, nxt2=True):
                g = i * UNROLL + j
                scores(g, j % 2)
                for b in range(GB):
                    product_v(g, j % 2, b)
                if nxt:
                    pe.wait_ge(hT_emptied, GB * g + 2 * GB)
                for c in range(K):
                    if nxt:
                        product_t(g + 1, (j + 1) % 2, c)
                    if nxt2:
                        transpose_h(g + 2, c)
                for b in range(GB):
                    product_out(g, b)

            def product_m(c):
                for k in range(K):
                    last = nc.tensor.matmul(bank[c][:], wqT[:, k, c], wkT[:, k], start=k == 0,
                                            stop=k == K - 1)
                last.then_inc(filled, 1)

            pe.wait_ge(ident_made, 1)
            for r in range(K):
                pe.wait_ge(wq_loaded[r], 16)
                for k in range(K):
                    last = nc.tensor.transpose(bank[r][:, k * N:(k + 1) * N], wq_sb[:, r, k * N:(k + 1) * N], ident[:])
                last.then_inc(wT_filled, 1)
                pe.wait_ge(wk_loaded[r], 16)
                for k in range(K):
                    last = nc.tensor.transpose(start_bank[r][:, k], wk_sb[:, r, k * N:(k + 1) * N], ident[:])
                last.then_inc(wT_filled, 1)
            pe.wait_ge(wT_copied_act, K)
            pe.wait_ge(wT_copied_vec, K)
            product_m(0)
            product_m(1)
            product_m(2)
            transpose_h(0, 0)
            transpose_h(0, 1)
            product_m(3)
            transpose_h(0, 2)
            transpose_h(0, 3)
            pe.wait_ge(w_split, K)
            for b in range(GB):
                pe.wait_ge(hT_emptied, b + 1)
                product_v(0, 0, b)
            for c in range(K):
                product_t(0, 0, c)
                if c < 2:
                    transpose_h(1, c)
            transpose_h(1, 2)
            transpose_h(1, 3)
            pe.wait_ge(ident_bf_made, 1)
            scores(0, 0)
            pe.wait_ge(hT_emptied, 2 * GB)
            for c in range(K):
                product_t(1, 1, c)
                transpose_h(2, c)
            for b in range(GB):
                product_out(0, b)
            with pe.Fori(0, TURNS) as i:
                for j in range(1, UNROLL + 1):
                    group(i + j // UNROLL, j % UNROLL)
            for g in REST:
                group(g // UNROLL, g % UNROLL, nxt=g + 1 < G, nxt2=g + 2 < G)


_INS = ["x", "adj", "L0_gnn_weight", "L0_gnn_wq", "L0_gnn_wk"]


def kernel(**inputs):
    import numpy as _np
    import concourse.bacc as _bacc
    from concourse import mybir as _mybir
    from concourse.bass_utils import run_bass_kernel_spmd as _run

    nc = _bacc.Bacc("TRN2", target_bir_lowering=False, num_devices=1)
    arrays, args = {}, []
    for name in _INS:
        a = _np.ascontiguousarray(inputs[name])
        arrays[f"in_{name}"] = a
        args.append(nc.dram_tensor(f"in_{name}", a.shape, _mybir.dt.from_np(a.dtype), kind="ExternalInput").ap())
    shape = inputs["x"].shape
    args.append(nc.dram_tensor("out_h", shape, _mybir.dt.float32, kind="ExternalOutput").ap())
    graph_attention_kernel(nc, *args)
    r = _run(nc, [arrays], core_ids=[0])
    return r.results[0]["out_h"]
```
